# Optimizing a Trainium2 kernel written in Bass

```python
import numpy as np
import jax
import jax.numpy as jnp

def _softmax(x, axis=-1):
    return jax.nn.softmax(x, axis=axis)

def _gelu(x):
    return jax.nn.gelu(x, approximate=True)

def _silu(x):
    return jax.nn.silu(x)

def _sigmoid(x):
    return jax.nn.sigmoid(x)

def _layernorm(x, axis=-1, eps=1e-05):
    m = jnp.mean(x, axis=axis, keepdims=True)
    v = jnp.var(x, axis=axis, keepdims=True)
    return (x - m) / jnp.sqrt(v + eps)

def _scatter_add(tgt, idx, src, axis=0):
    return tgt.at[idx].add(src)

def _segment_sum(src, seg, n):
    return jax.ops.segment_sum(src, seg, n)
kernel_name = 'mk_gnn_resnorm_d1_gnn_r8_5553ed'

def setup_inputs(seed: int=0):
    np.random.seed(seed)
    _w = jnp.asarray

    def _rec_inputs():
        import jax
        import jax.numpy as jnp
        _gk = jax.random.key(seed)
        x = -8.776e-05 + 1 * jax.random.normal(jax.random.fold_in(_gk, 1), (1250, 512), jnp.float32)
        src = jax.random.randint(jax.random.fold_in(_gk, 2), (40000,), 0, 1250, jnp.int32)
        dst = jnp.minimum((1250 * jax.random.uniform(jax.random.fold_in(_gk, 3), (40000,)) ** 2.0).astype(jnp.int32), 9999)
        _o = jnp.argsort(dst, stable=True)
        src = src[_o]
        dst = dst[_o]
        return (x, src, dst)
    x, src, dst = _rec_inputs()

    def _L0_gnn_setup():
        import jax, jax.numpy as jnp
        import numpy as np
        N_NODES = 1250
        N_EDGES = 20000
        DIM = 512
        LN_EPS = 1e-05
        key = jax.random.key(seed)
        ks = jax.random.split(key, 6)
        scale = 1.0 / np.sqrt(DIM)
        h = jax.random.normal(ks[0], (N_NODES, DIM), dtype=jnp.float32)
        edge_index = jax.random.randint(ks[1], (2, N_EDGES), 0, N_NODES, dtype=jnp.int32)
        W_self = jax.random.normal(ks[2], (DIM, DIM), dtype=jnp.float32) * scale
        b_self = jnp.zeros((DIM,), dtype=jnp.float32)
        W_neigh = jax.random.normal(ks[3], (DIM, DIM), dtype=jnp.float32) * scale
        b_neigh = jnp.zeros((DIM,), dtype=jnp.float32)
        ln_gamma = jnp.ones((DIM,), dtype=jnp.float32)
        ln_beta = jnp.zeros((DIM,), dtype=jnp.float32)
        return {'h': h, 'edge_index': edge_index, 'W_self': W_self, 'b_self': b_self, 'W_neigh': W_neigh, 'b_neigh': b_neigh, 'ln_gamma': ln_gamma, 'ln_beta': ln_beta}
    _L0_gnn_all = _L0_gnn_setup()
    _L0_gnn_in = {k: v for k, v in _L0_gnn_all.items() if k in ('W_self', 'b_self', 'W_neigh', 'b_neigh', 'ln_gamma', 'ln_beta')}
    del _L0_gnn_all
    return {'x': x, 'src': src, 'dst': dst, 'L0_gnn_W_self': _L0_gnn_in['W_self'], 'L0_gnn_b_self': _L0_gnn_in['b_self'], 'L0_gnn_W_neigh': _L0_gnn_in['W_neigh'], 'L0_gnn_b_neigh': _L0_gnn_in['b_neigh'], 'L0_gnn_ln_gamma': _L0_gnn_in['ln_gamma'], 'L0_gnn_ln_beta': _L0_gnn_in['ln_beta']}

def reference(x, src, dst, L0_gnn_W_self, L0_gnn_b_self, L0_gnn_W_neigh, L0_gnn_b_neigh, L0_gnn_ln_gamma, L0_gnn_ln_beta):
    import jax
    import jax.numpy as jnp

    def _L0_gnn_ref(h, edge_index, W_self, b_self, W_neigh, b_neigh, ln_gamma, ln_beta):
        import jax, jax.numpy as jnp
        import numpy as np
        N_NODES = 1250
        N_EDGES = 20000
        DIM = 512
        LN_EPS = 1e-05
        n = h.shape[0]
        src = edge_index[0]
        dst = edge_index[1]
        msg = h[dst] @ W_neigh.T + b_neigh
        neigh = jax.ops.segment_sum(msg, src, num_segments=n)
        deg = jax.ops.segment_sum(jnp.ones(src.shape, h.dtype), src, num_segments=n)
        deg = jnp.maximum(deg, 1.0)
        neigh = neigh / deg[:, None]
        out = jax.nn.relu(h @ W_self.T + b_self + neigh)
        x = h + out
        mean = jnp.mean(x, axis=-1, keepdims=True)
        var = jnp.mean(jnp.square(x - mean), axis=-1, keepdims=True)
        return (x - mean) * jax.lax.rsqrt(var + LN_EPS) * ln_gamma + ln_beta
    edge_index = jnp.stack([src, dst])
    x = _layernorm(x + _L0_gnn_ref(x, edge_index, L0_gnn_W_self, L0_gnn_b_self, L0_gnn_W_neigh, L0_gnn_b_neigh, L0_gnn_ln_gamma, L0_gnn_ln_beta), axis=-1)
    return x

_drawn_inputs = setup_inputs


def setup_inputs(seed=0):
    import zlib

    import numpy as np

    out = dict(_drawn_inputs(seed))
    spreads = {'L0_gnn_b_self': (0.0, 0.1),
     'L0_gnn_b_neigh': (0.0, 0.1),
     'L0_gnn_ln_gamma': (1.0, 0.2),
     'L0_gnn_ln_beta': (0.0, 0.1)}
    factors = {}
    for name, (base, spread) in spreads.items():
        noise = np.random.default_rng([zlib.crc32(name.encode()), seed]).standard_normal(out[name].shape)
        drawn = base * np.exp(spread * noise) if base else spread * noise
        out[name] = jnp.asarray(drawn.astype(out[name].dtype))
    for name, factor in factors.items():
        out[name] = (out[name] * factor).astype(out[name].dtype)
    return out
```

```python
from contextlib import ExitStack

import numpy as np

import concourse.bass as bass
from concourse import mybir

NODES, DIM, EDGES = 1250, 512, 40000
P = 125
TILES = NODES // P
CHUNKS = EDGES // P
GROUP = 4
WIN = 25
WPT = P // WIN
WINDOWS = NODES // WIN
COLS = WIN * TILES
CROWS, CBLK = 80, 4
KT = DIM // 128
SLOTS = 4
LHS = 128
EPS = 1e-5
FAR = 4096.0
ROUND = 12582912.0


def build(nc, dst_rows, dst, src, xT, x, wn, ws, bn, bs, gamma, beta, out):
    fp32, f32r, bf16, i32, f8 = (mybir.dt.float32, mybir.dt.float32r, mybir.dt.bfloat16,
                                 mybir.dt.int32, mybir.dt.float8e4)
    ALU, ACT, AX = mybir.AluOpType, mybir.ActivationFunctionType, mybir.AxisListType

    ctx = ExitStack()
    with ctx:
        def sb(name, shape, dt):
            return ctx.enter_context(nc.sbuf_tensor(name, shape, dt))

        def ps(name, shape, dt=fp32):
            return ctx.enter_context(nc.psum_tensor(name, shape, dt))

        def sem(name):
            return ctx.enter_context(nc.semaphore(name))

        counts_T = sb("counts_T", [P, TILES, NODES], f32r)
        counts_rest = sb("counts_rest", [P, TILES, NODES], f8)
        y_hi = sb("y_hi", [P, TILES, DIM], f32r)
        y_lo = sb("y_lo", [P, TILES, DIM], f32r)
        z = sb("z", [P, TILES, DIM], fp32)
        xT_sb = sb("xT_sb", [128, KT, NODES], fp32)
        wn_sb = sb("wn_sb", [128, KT, DIM], fp32)
        ws_sb = sb("ws_sb", [128, KT, DIM], fp32)
        counts = sb("counts", [P, 2, TILES, P], fp32)
        counts_T32 = sb("counts_T32", [P, NODES], fp32)
        y32 = sb("y32", [P, DIM], fp32)
        oh_b = sb("oh_b", [P, SLOTS, GROUP, LHS], bf16)
        oh_da = sb("oh_da", [P, SLOTS, GROUP, COLS], bf16)
        keys = sb("keys", [P, CHUNKS + GROUP, 2], fp32)
        stage = sb("stage", [P, SLOTS, GROUP, 2], fp32)
        cols = sb("cols", [P, COLS], bf16)
        win_start = sb("win_start", [P, WINDOWS, 2], fp32)
        bn_sb = sb("bn_sb", [P, DIM], fp32)
        bs_sb = sb("bs_sb", [P, DIM], fp32)
        gamma_sb = sb("gamma_sb", [P, DIM], fp32)
        beta_sb = sb("beta_sb", [P, DIM], fp32)
        ident = sb("ident", [128, 128], fp32)
        ones_r = sb("ones_r", [P, 2], f32r)
        small = sb("small", [P, 96], fp32)
        table = sb("table", [1, WINDOWS, 4], i32)
        flag_i = sb("flag_i", [1, 4], i32)
        zeros = sb("zeros", [P, LHS], bf16)

        dst_i = z[:, 9, 0:CHUNKS].bitcast(i32)
        src_i = z[:, 8, 0:CHUNKS].bitcast(i32)
        dst_ci = z[0:CROWS, 7, 0:CBLK * P].bitcast(i32)
        dst_f, src_f, a_f = z[:, 6, 0:CHUNKS], z[:, 5, 0:CHUNKS], z[:, 4, 0:CHUNKS]
        diag_lo = z[0:CROWS, 3, 0:CHUNKS]
        diag_hi = z[0:CROWS, 2, 0:CHUNKS]
        late = z[0:WINDOWS, 1, 0:CHUNKS]
        miss = z[0:WINDOWS, 0, 0:CHUNKS]
        lo_c = counts[0:WINDOWS, 0, 0:3, :].rearrange("p a d -> p (a d)")[:, 0:CHUNKS]
        hi_c = counts[0:WINDOWS, 0, 4:7, :].rearrange("p a d -> p (a d)")[:, 0:CHUNKS]
        chunk_no = counts[0:WINDOWS, 1, 0:3, :].rearrange("p a d -> p (a d)")[:, 0:CHUNKS]
        before = counts[0:WINDOWS, 1, 4, 0:WINDOWS + 1]
        ones80 = counts[0:CROWS, 1, 5, 0:WINDOWS]

        def work(n):
            return xT_sb[0:P, n // 2, (n % 2) * 576:(n % 2) * 576 + DIM]
        x_t = [work(0), work(1)]
        h_t = [work(2), work(3)]
        g_t = [work(4), work(5)]
        xb_t = [work(6), work(7)]
        o_t = [ws_sb[0:P, 0, :], ws_sb[0:P, 1, :]]
        n_t = [ws_sb[0:P, 2, :], ws_sb[0:P, 3, :]]
        rest_r = sb("rest_r", [P, TILES, P], f32r)

        ps_win = [ps("ps_win0", [128, 512]), ps("ps_win1", [128, 512])]
        ps_dense = ps("ps_dense", [128, 512])
        ps_tr = [ps("ps_tr0", [128, 512]), ps("ps_tr1", [128, 512])]
        ps_deg = ps("ps_deg", [128, 512])
        ps_out = [ps("ps_out0", [128, 512]), ps("ps_out1", [128, 512])]

        edges_in = sem("edges_in")
        w_in = sem("w_in")
        ws_in = sem("ws_in")
        vec_in = sem("vec_in")
        x_in = [sem("x_in0"), sem("x_in1")]
        consts = sem("consts")
        dve_step = sem("dve_step")
        diag_ready = sem("diag_ready")
        spread_ready = sem("spread_ready")
        ranges_ready = sem("ranges_ready")
        rows_ready = sem("rows_ready")
        table_ready = sem("table_ready")
        staged = sem("staged")
        group_ready = sem("group_ready")
        group_used = sem("group_used")
        win_done = sem("win_done")
        win_out = sem("win_out")
        dense_done = sem("dense_done")
        z_out = sem("z_out")
        tr_done = sem("tr_done")
        tr_out = sem("tr_out")
        t32_out = sem("t32_out")
        rest_done = sem("rest_done")
        y32_ready = sem("y32_ready")
        y32_biased = sem("y32_biased")
        y_hi_ready = sem("y_hi_ready")
        y_ready = sem("y_ready")
        z_ready = sem("z_ready")
        deg_ready = sem("deg_ready")
        over_ready = sem("over_ready")
        over_sum = sem("over_sum")
        flag_ready = sem("flag_ready")
        rest_cast = sem("rest_cast")
        rest_used = sem("rest_used")
        out_done = sem("out_done")
        var1 = sem("var1")
        std1 = sem("std1")
        stat1 = sem("stat1")
        norm1 = sem("norm1")
        xb_ready = sem("xb_ready")
        scaled = sem("scaled")
        pool_step = sem("pool_step")
        g_ready = sem("g_ready")
        var2 = sem("var2")
        std2 = sem("std2")
        stat2 = sem("stat2")
        o_ready = sem("o_ready")
        stored = [sem("stored0"), sem("stored1")]
        const_step = sem("const_step")

        def S(c, n=1, rows=P):
            return small[0:rows, c:c + n]
        LO, HI, NUM, T0, EPSC = 0, 1, 2, 3, 4
        CMIN, CMAX = 8, 12
        WLO, WHI, ONE = 5, 6, 7
        R, MV1, MV2, STD, RSTD, NB = 16, 18, 22, 26, 28, 30
        ST = 36
        OVER = 60

        block = ctx.enter_context(nc.Block())

        @block.sync
        def _(sp):
            sp.dma_start(dst_ci, dst_rows).then_inc(edges_in, 16)
            sp.dma_start(dst_i, dst).then_inc(edges_in, 16)
            sp.dma_start(src_i, src).then_inc(edges_in, 16)
            sp.dma_start(wn_sb[:, :, :], wn.rearrange("(k p) n -> p k n", p=128)).then_inc(w_in, 16)
            sp.dma_start(xT_sb[:, :, :], xT.rearrange("(k p) n -> p k n", p=128)).then_inc(w_in, 16)
            sp.dma_start(bn_sb[:, :], bn.partition_broadcast(P)).then_inc(vec_in, 16)
            sp.dma_start(ws_sb[:, :, :], ws.rearrange("(k p) n -> p k n", p=128)).then_inc(ws_in, 16)
            sp.dma_start(bs_sb[:, :], bs.partition_broadcast(P)).then_inc(vec_in, 16)
            sp.dma_start(gamma_sb[:, :], gamma.partition_broadcast(P)).then_inc(vec_in, 16)
            sp.dma_start(beta_sb[:, :], beta.partition_broadcast(P)).then_inc(vec_in, 16)
            sp.wait_ge(dense_done, 2 * TILES)
            for a in range(TILES):
                if a >= 2:
                    sp.wait_ge(xb_ready, a - 1)
                    sp.wait_ge(var1, a - 1)
                sp.dma_start(x_t[a % 2], x[a * P:(a + 1) * P, :]).then_inc(x_in[a % 2], 16)
                if a >= 2:
                    sp.wait_ge(o_ready, a - 1)
                    sp.dma_start(out[(a - 2) * P:(a - 1) * P, :], o_t[a % 2]).then_inc(stored[a % 2], 16)
            for a in range(TILES - 2, TILES):
                sp.wait_ge(o_ready, a + 1)
                sp.dma_start(out[a * P:(a + 1) * P, :], o_t[a % 2]).then_inc(stored[a % 2], 16)
            sp.wait_ge(stored[0], 16 * TILES // 2)
            sp.wait_ge(stored[1], 16 * TILES // 2)

        @block.gpsimd
        def _(pool):
            pool.memset(ident[:, :], 0.0).then_inc(const_step, 1)
            pool.memset(before, 1.0).then_inc(const_step, 1)
            pool.iota(cols[:, :], [[1, COLS]], base=0, channel_multiplier=0,
                      allow_small_or_imprecise_dtypes=True)
            pool.iota(chunk_no, [[1, CHUNKS]], base=0, channel_multiplier=0,
                      allow_small_or_imprecise_dtypes=True)
            pool.iota(win_start[:, :, 0], [[COLS, WINDOWS]], base=0, channel_multiplier=0,
                      allow_small_or_imprecise_dtypes=True)
            pool.iota(S(WLO, 1, WINDOWS), [[1, 1]], base=0, channel_multiplier=WIN,
                      allow_small_or_imprecise_dtypes=True)
            pool.iota(S(WHI, 1, WINDOWS), [[1, 1]], base=WIN - 1, channel_multiplier=WIN,
                      allow_small_or_imprecise_dtypes=True)
            pool.memset(win_start[:, :, 1], 0.0)
            pool.memset(ones80, 1.0)
            pool.memset(zeros[:, :], 0.0)
            pool.memset(S(EPSC), EPS)
            pool.memset(S(ONE), 1.0)
            pool.memset(keys[:, CHUNKS:, :], -FAR)
            pool.wait_ge(const_step, 2)
            pool.affine_select(out=before, in_=before, compare_op=ALU.is_gt, fill=0.0, base=0,
                               pattern=[[1, WINDOWS + 1]], channel_multiplier=-1)
            pool.affine_select(out=ident[:, :], in_=ident[:, :], compare_op=ALU.not_equal, fill=1.0,
                               base=0, pattern=[[-1, 128]], channel_multiplier=1).then_inc(consts, 1)
            pool.wait_ge(vec_in, 64)
            for i in range(TILES):
                pool.wait_ge(y32_ready, i + 1)
                pool.tensor_tensor(y32[:, :], y32[:, :], bn_sb[:, :], ALU.add).then_inc(y32_biased, 1)
                pool.wait_ge(y_hi_ready, i + 1)
                pool.tensor_tensor(y_lo[:, i, :], y32[:, :], y_hi[:, i, :].bitcast(fp32), ALU.subtract).then_inc(y_ready, 1)
                pool.wait_ge(z_out, i + 1)
                pool.tensor_tensor(z[:, i, :], z[:, i, :], bs_sb[:, :], ALU.add).then_inc(z_ready, 1)
                if i >= 1:
                    pool.wait_ge(t32_out, 3 * i)
                    pool.tensor_tensor(counts_rest[:, i - 1, :], counts_T32[:, :],
                                       counts_T[:, i - 1, :].bitcast(fp32), ALU.subtract,
                                       saturate=False).then_inc(rest_done, 1)
            pool.wait_ge(t32_out, 3 * TILES)
            pool.tensor_tensor(counts_rest[:, TILES - 1, :], counts_T32[:, :],
                               counts_T[:, TILES - 1, :].bitcast(fp32), ALU.subtract,
                                       saturate=False).then_inc(rest_done, 1)
            for a in range(TILES):
                p = a % 2
                pool.wait_ge(x_in[p], 16 * (a // 2 + 1))
                if a >= 2:
                    pool.wait_ge(g_ready, a - 1)
                pool.tensor_tensor(xb_t[p], x_t[p], beta_sb[:, :], ALU.add).then_inc(xb_ready, 1)
                pool.wait_ge(norm1, a + 1)
                pool.tensor_tensor(n_t[p], n_t[p], gamma_sb[:, :], ALU.mult).then_inc(scaled, 1)
                pool.wait_ge(scaled, a + 1)
                if a >= 2:
                    pool.wait_ge(o_ready, a - 1)
                pool.tensor_tensor(g_t[p], n_t[p], xb_t[p], ALU.add).then_inc(g_ready, 1)

        @block.scalar
        def _(act):
            def window_out(j):
                i, w = j // WPT, j % WPT
                act.wait_ge(win_done, j + 1)
                if w == 0 and i >= 2:
                    act.wait_ge(tr_done, 3 * (i - 1))
                act.activation(counts[:, i % 2, :, w * WIN:(w + 1) * WIN],
                               ps_win[j % 2][0:P, 0:COLS].rearrange("p (d a) -> p a d", a=TILES),
                               ACT.Copy).then_inc(win_out, 1)

            def transposed_out(i, batch):
                n = min(4, TILES - 4 * batch)
                act.wait_ge(tr_done, 3 * i + batch + 1)
                source = ps_tr[batch % 2][0:P, 0:n * 128].rearrange("p (a s) -> p a s", s=128)[:, :, 0:P]
                act.activation(counts_T[:, i, 4 * batch * P:(4 * batch + n) * P].rearrange("p (a s) -> p a s", s=P),
                               source, ACT.Copy).then_inc(tr_out, 1)
                if i >= 1 and batch == 0:
                    act.wait_ge(rest_done, i)
                act.activation(counts_T32[:, 4 * batch * P:(4 * batch + n) * P].rearrange("p (a s) -> p a s", s=P),
                               source, ACT.Copy).then_inc(t32_out, 1)

            act.wait_ge(table_ready, 1)
            for i in range(TILES):
                for w in range(WPT):
                    if w == 1:
                        act.wait_ge(dense_done, 2 * i + 1)
                        if i >= 1:
                            act.wait_ge(y_ready, i)
                        act.activation(y32[:, :], ps_dense[0:P, :], ACT.Copy).then_inc(y32_ready, 1)
                    if w == 3:
                        act.wait_ge(dense_done, 2 * i + 2)
                        act.activation(z[:, i, :], ps_dense[0:P, :], ACT.Copy).then_inc(z_out, 1)
                    window_out(WPT * i + w)
                    if w == 2:
                        act.wait_ge(y32_biased, i + 1)
                        act.activation(y_hi[:, i, :], y32[:, :], ACT.Copy).then_inc(y_hi_ready, 1)
                    if w == 4 and i >= 1:
                        for batch in range(3):
                            transposed_out(i - 1, batch)
            for batch in range(3):
                transposed_out(TILES - 1, batch)
            for a in range(TILES + 1):
                if a < TILES:
                    p = a % 2
                    act.wait_ge(var1, a + 1)
                    act.activation(S(STD + p), S(MV1 + 2 * p + 1), ACT.Sqrt, bias=S(EPSC)).then_inc(std1, 1)
                    act.wait_ge(stat1, a + 1)
                    if a >= 2:
                        act.wait_ge(g_ready, a - 1)
                    act.activation(n_t[p], h_t[p], ACT.Identity, scale=S(RSTD + p), bias=S(NB + p)).then_inc(norm1, 1)
                if a >= 1:
                    q = (a - 1) % 2
                    act.wait_ge(var2, a)
                    act.activation(S(STD + 40 + q), S(MV2 + 2 * q + 1), ACT.Sqrt, bias=S(EPSC)).then_inc(std2, 1)
                    act.wait_ge(stat2, a)
                    if a >= 3:
                        act.wait_ge(stored[q], 16 * ((a - 1) // 2))
                    act.activation(o_t[q], g_t[q], ACT.Identity, scale=S(RSTD + 40 + q), bias=S(NB + 40 + q)).then_inc(o_ready, 1)

        @block.vector
        def _(dve):
            step = [0]

            def link(ins):
                step[0] += 1
                ins.then_inc(dve_step, 1)
                dve.wait_ge(dve_step, step[0])

            dve.wait_ge(edges_in, 48)
            rows = dst_ci.rearrange("p (t e) -> p t e", e=P)
            dve.tensor_reduce(out=S(CMIN, CBLK, CROWS), in_=rows, op=ALU.min, axis=AX.X)
            link(dve.tensor_reduce(out=S(CMAX, CBLK, CROWS), in_=rows, op=ALU.max, axis=AX.X))
            dve.wait_ge(consts, 1)
            eye = ident[0:CROWS, 0:CROWS]
            for t in range(CBLK):
                dve.tensor_scalar(diag_lo[:, t * CROWS:(t + 1) * CROWS], eye, S(CMIN + t, 1, CROWS), None, ALU.mult)
                last = dve.tensor_scalar(diag_hi[:, t * CROWS:(t + 1) * CROWS], eye, S(CMAX + t, 1, CROWS), None, ALU.mult)
            last.then_inc(diag_ready, 1)
            dve.tensor_copy(src_f, src_i)
            link(dve.tensor_copy(dst_f, dst_i))
            link(dve.tensor_scalar(a_f, src_f, -(P - 1) / 2.0, 1.0 / P, ALU.add, ALU.mult))
            link(dve.tensor_scalar(a_f, a_f, ROUND, -ROUND, ALU.add, ALU.add))
            dve.scalar_tensor_tensor(out=keys[:, 0:CHUNKS, 1], in0=a_f, scalar=-float(P), in1=src_f, op0=ALU.mult, op1=ALU.add)
            dve.scalar_tensor_tensor(out=keys[:, 0:CHUNKS, 0], in0=dst_f, scalar=float(TILES), in1=a_f, op0=ALU.mult, op1=ALU.add)
            dve.wait_ge(spread_ready, 2)
            least, most = ps_out[0][0:WINDOWS, 0:CHUNKS], ps_out[1][0:WINDOWS, 0:CHUNKS]
            link(dve.tensor_scalar(late, least, S(WHI, 1, WINDOWS), None, ALU.is_gt))
            link(dve.scalar_tensor_tensor(out=miss, in0=most, scalar=S(WLO, 1, WINDOWS), in1=late, op0=ALU.is_lt, op1=ALU.add))
            dve.scalar_tensor_tensor(out=lo_c, in0=miss, scalar=FAR, in1=chunk_no, op0=ALU.mult, op1=ALU.add)
            link(dve.scalar_tensor_tensor(out=hi_c, in0=miss, scalar=-FAR, in1=chunk_no, op0=ALU.mult, op1=ALU.add))
            dve.tensor_reduce(out=S(LO, 1, WINDOWS), in_=lo_c, op=ALU.min, axis=AX.X)
            link(dve.tensor_reduce(out=S(HI, 1, WINDOWS), in_=hi_c, op=ALU.max, axis=AX.X))
            link(dve.tensor_tensor(S(T0, 1, WINDOWS), S(HI, 1, WINDOWS), S(LO, 1, WINDOWS), ALU.subtract))
            link(dve.tensor_scalar(S(T0, 1, WINDOWS), S(T0, 1, WINDOWS), GROUP - (GROUP - 1) / 2.0, 1.0 / GROUP, ALU.add, ALU.mult))
            link(dve.tensor_scalar(S(T0, 1, WINDOWS), S(T0, 1, WINDOWS), ROUND, -ROUND, ALU.add, ALU.add))
            dve.tensor_scalar(S(NUM, 1, WINDOWS), S(T0, 1, WINDOWS), 1.0, None, ALU.max)
            dve.tensor_scalar(S(LO, 1, WINDOWS), S(LO, 1, WINDOWS), CHUNKS - 1.0, None, ALU.min).then_inc(ranges_ready, 1)
            dve.wait_ge(rows_ready, 1)
            dve.tensor_copy(table[:, :, 0], ps_out[0][0:1, 0:WINDOWS])
            dve.tensor_copy(table[:, :, 1], ps_out[0][0:1, 1:WINDOWS + 1])
            link(dve.tensor_copy(table[:, :, 2], ps_out[0][0:1, 64:64 + WINDOWS]))
            dve.memset(ones_r[:, :].bitcast(fp32), 1.0).then_inc(table_ready, 1)

            dve.wait_ge(dve_step, step[0])
            with dve.Fori(0, WINDOWS) as j:
                g0 = dve.value_load(table[0:1, j, 0:1], min_val=0, max_val=WINDOWS * CHUNKS)
                g1 = dve.value_load(table[0:1, j, 1:2], min_val=1, max_val=WINDOWS * CHUNKS)
                c0 = dve.value_load(table[0:1, j, 2:3], min_val=0, max_val=CHUNKS - 1)
                with dve.Fori(g0, g1) as g:
                    c = dve.snap(((g - g0) * GROUP + c0).with_bounds(min_val=0, max_val=CHUNKS - 1))
                    slot = dve.snap(g % SLOTS)
                    dve.wait_ge(group_used, g + 1)
                    dve.tensor_tensor(stage[:, bass.ds(slot, 1), :, :], keys[:, bass.ds(c, GROUP), :],
                                      win_start[:, bass.ds(j, 1), :].broadcast_to([P, GROUP, 2]),
                                      ALU.subtract).then_inc(staged, 1)
                    dve.wait_ge(staged, g + 1)
                    for q in range(GROUP):
                        dve.tensor_scalar(oh_b[:, bass.ds(slot, 1), q, :], cols[:, 0:LHS], stage[:, bass.ds(slot, 1), q, 1:2], None, ALU.is_equal)
                        last = dve.tensor_scalar(oh_da[:, bass.ds(slot, 1), q, :], cols[:, :], stage[:, bass.ds(slot, 1), q, 0:1], None, ALU.is_equal)
                    last.then_inc(group_ready, 1)

            dve.wait_ge(deg_ready, TILES)
            link(dve.tensor_reduce(out=S(OVER), in_=ps_deg[0:P, 0:2 * TILES], op=ALU.max, axis=AX.X))
            dve.tensor_scalar(S(OVER + 1), S(OVER), FAR, None, ALU.is_ge).then_inc(over_ready, 1)
            dve.wait_ge(over_sum, 1)
            dve.tensor_copy(flag_i[0:1, 0:1], ps_win[0][0:1, 0:1]).then_inc(flag_ready, 1)
            dve.wait_ge(flag_ready, 1)
            over = dve.value_load(flag_i[0:1, 0:1], min_val=0, max_val=P)
            dve.wait_ge(z_ready, TILES)
            dve.wait_ge(rest_done, TILES)
            for a in range(TILES + 1):
                if a < TILES:
                    p = a % 2
                    with dve.If(over > 0):
                        if a >= 1:
                            dve.wait_ge(rest_used, a)
                        dve.tensor_copy(rest_r[:, :, :], counts_rest[:, :, a * P:(a + 1) * P]).then_inc(rest_cast, 1)
                    dve.wait_ge(out_done, a + 1)
                    link(dve.tensor_scalar(S(R + p), ps_deg[0:P, 2 * a:2 * a + 1], 1.0, None, ALU.max))
                    link(dve.reciprocal(S(R + p), S(R + p)))
                    if a >= 2:
                        dve.wait_ge(norm1, a - 1)
                    link(dve.scalar_tensor_tensor(out=h_t[p], in0=ps_out[p][0:P, :], scalar=S(R + p), in1=z[:, a, :],
                                                  op0=ALU.mult, op1=ALU.add))
                    dve.wait_ge(x_in[p], 16 * (a // 2 + 1))
                    link(dve.scalar_tensor_tensor(out=h_t[p], in0=h_t[p], scalar=0.0, in1=x_t[p], op0=ALU.max, op1=ALU.add))
                    link(dve.bn_stats(S(ST + 6 * p, 6), h_t[p]))
                    dve.bn_aggr(S(MV1 + 2 * p, 2), S(ST + 6 * p, 6)).then_inc(var1, 1)
                    dve.wait_ge(std1, a + 1)
                    link(dve.reciprocal(S(RSTD + p), S(STD + p)))
                    dve.scalar_tensor_tensor(out=S(NB + p), in0=S(MV1 + 2 * p), scalar=-1.0, in1=S(RSTD + p),
                                             op0=ALU.mult, op1=ALU.mult).then_inc(stat1, 1)
                if a >= 1:
                    q = (a - 1) % 2
                    dve.wait_ge(g_ready, a)
                    link(dve.bn_stats(S(ST + 12 + 6 * q, 6), g_t[q]))
                    dve.bn_aggr(S(MV2 + 2 * q, 2), S(ST + 12 + 6 * q, 6)).then_inc(var2, 1)
                    dve.wait_ge(std2, a)
                    link(dve.reciprocal(S(RSTD + 40 + q), S(STD + 40 + q)))
                    dve.scalar_tensor_tensor(out=S(NB + 40 + q), in0=S(MV2 + 2 * q), scalar=-1.0, in1=S(RSTD + 40 + q),
                                             op0=ALU.mult, op1=ALU.mult).then_inc(stat2, 1)

        @block.tensor
        def _(pe):
            pe.wait_ge(diag_ready, 1)
            pe.matmul(ps_out[0][0:WINDOWS, 0:CHUNKS], ones80, diag_lo, start=True, stop=True).then_inc(spread_ready, 1)
            pe.matmul(ps_out[1][0:WINDOWS, 0:CHUNKS], ones80, diag_hi, start=True, stop=True).then_inc(spread_ready, 1)
            pe.wait_ge(ranges_ready, 1)
            pe.matmul(ps_out[0][0:1, 0:WINDOWS + 1], S(NUM, 1, WINDOWS), before, start=True, stop=True)
            pe.matmul(ps_out[0][0:1, 64:64 + WINDOWS], S(LO, 1, WINDOWS), ident[0:WINDOWS, 0:WINDOWS],
                      start=True, stop=True).then_inc(rows_ready, 1)
            pe.sem_inc(group_used, SLOTS)
            pe.wait_ge(w_in, 32)
            pe.wait_ge(table_ready, 1)

            def dense(i, which, k):
                if k == 0 and which == 1:
                    pe.wait_ge(y32_ready, i + 1)
                if k == 0 and which == 0 and i >= 1:
                    pe.wait_ge(z_out, i)
                if i == 0 and which == 1 and k == 0:
                    pe.wait_ge(ws_in, 16)
                w = (wn_sb, ws_sb)[which]
                m = pe.matmul(ps_dense[0:P, :], xT_sb[:, k, i * P:(i + 1) * P], w[:, k, :],
                              start=k == 0, stop=k == KT - 1)
                if k == KT - 1:
                    m.then_inc(dense_done, 1)

            def transposes(i, batch):
                if batch == 0:
                    pe.wait_ge(win_out, WPT * (i + 1))
                if batch == 2 or i >= 1:
                    pe.wait_ge(t32_out, 3 * i + batch - (0, 2, 1)[batch])
                for a in range(4 * batch, min(4 * batch + 4, TILES)):
                    last = pe.transpose(ps_tr[batch % 2][0:P, (a % 4) * 128:(a % 4) * 128 + P],
                                        counts[:, i % 2, a, :], ident[0:P, 0:P])
                last.then_inc(tr_done, 1)

            def degrees(i):
                pe.wait_ge(tr_out, 3 * (i + 1))
                for a in range(TILES):
                    last = pe.matmul(ps_deg[0:P, 2 * a:2 * a + 2], counts_T[:, i, a * P:(a + 1) * P], ones_r[:, :],
                                     start=i == 0 and a == 0, stop=i == TILES - 1, skip_group_check=True)
                last.then_inc(deg_ready, 1)

            for i in range(TILES):
                for w in range(WPT):
                    j = WPT * i + w
                    if w < 4:
                        dense(i, w // 2, 2 * (w % 2))
                        dense(i, w // 2, 2 * (w % 2) + 1)
                    if w == 2 and i >= 2:
                        degrees(i - 2)
                    if w == 4 and i >= 1:
                        transposes(i - 1, 0)
                        transposes(i - 1, 1)
                    if j >= 2:
                        pe.wait_ge(win_out, j - 1)
                    bank = ps_win[j % 2]
                    pe.matmul(bank[:, COLS:COLS + 2], zeros[:, :], zeros[:, 0:2], start=True, stop=False,
                              skip_group_check=True)
                    g0 = pe.value_load(table[0:1, j, 0:1], min_val=0, max_val=WINDOWS * CHUNKS)
                    g1 = pe.value_load(table[0:1, j, 1:2], min_val=1, max_val=WINDOWS * CHUNKS)
                    with pe.Fori(g0, g1) as g:
                        slot = pe.snap(g % SLOTS)
                        pe.wait_ge(group_ready, g + 1)
                        for q in range(GROUP):
                            last = pe.matmul(bank[:, 0:COLS], oh_b[:, bass.ds(slot, 1), q, :], oh_da[:, bass.ds(slot, 1), q, :],
                                             start=False, stop=False, skip_group_check=True)
                        last.then_inc(group_used, 1)
                    pe.matmul(bank[:, COLS:COLS + 2], zeros[:, :], zeros[:, 0:2], start=False, stop=True,
                              skip_group_check=True).then_inc(win_done, 1)
                    if w == 4 and i >= 1:
                        transposes(i - 1, 2)
            for batch in range(3):
                transposes(TILES - 1, batch)
            degrees(TILES - 2)
            degrees(TILES - 1)

            pe.wait_ge(y_ready, TILES)
            for a in range(TILES):
                if a >= 2:
                    pe.wait_ge(var1, a - 1)
                for i in range(TILES):
                    for part in (y_hi, y_lo):
                        last = pe.matmul(ps_out[a % 2][0:P, :], counts_T[:, i, a * P:(a + 1) * P], part[:, i, :],
                                         start=i == 0 and part is y_hi, stop=False, skip_group_check=True)
                if a == 0:
                    pe.wait_ge(over_ready, 1)
                    pe.matmul(ps_win[0][0:1, 0:1], S(OVER + 1), S(ONE), start=True, stop=True).then_inc(over_sum, 1)
                    pe.wait_ge(flag_ready, 1)
                    over = pe.value_load(flag_i[0:1, 0:1], min_val=0, max_val=P)
                with pe.If(over > 0):
                    pe.wait_ge(rest_cast, a + 1)
                    for i in range(TILES):
                        for part in (y_hi, y_lo):
                            pe.matmul(ps_out[a % 2][0:P, :], rest_r[:, i, :], part[:, i, :],
                                      start=False, stop=False, skip_group_check=True)
                        last = pe.matmul(ps_deg[0:P, 2 * a:2 * a + 2], rest_r[:, i, :], ones_r[:, :],
                                         start=False, stop=False, skip_group_check=True)
                    last.then_inc(rest_used, 1)
                pe.matmul(ps_out[a % 2][0:P, 0:2], zeros[:, 0:P], zeros[:, 0:2], start=False, stop=True,
                          skip_group_check=True).then_inc(out_done, 1)


def kernel(**inputs):
    import concourse.bacc as bacc
    from concourse.bass_utils import run_bass_kernel_spmd

    src = np.asarray(inputs["src"]).reshape(CHUNKS, P)
    dst = np.asarray(inputs["dst"]).reshape(CHUNKS, P)
    x = np.asarray(inputs["x"])
    arrays = {
        "dst_rows": dst.reshape(CBLK, CROWS, P).transpose(1, 0, 2).reshape(CROWS, CBLK * P),
        "dst": dst.T, "src": src.T, "xT": x.T, "x": x,
        "wn": np.asarray(inputs["L0_gnn_W_neigh"]).T, "ws": np.asarray(inputs["L0_gnn_W_self"]).T,
        "bn": inputs["L0_gnn_b_neigh"], "bs": inputs["L0_gnn_b_self"],
        "gamma": inputs["L0_gnn_ln_gamma"], "beta": inputs["L0_gnn_ln_beta"],
    }
    arrays = {n: np.ascontiguousarray(a) for n, a in arrays.items()}
    nc = bacc.Bacc("TRN2", target_bir_lowering=False, num_devices=1)
    args = {n: nc.dram_tensor(f"in_{n}", a.shape, mybir.dt.from_np(a.dtype), kind="ExternalInput").ap()
            for n, a in arrays.items()}
    out = nc.dram_tensor("out", (NODES, DIM), mybir.dt.float32, kind="ExternalOutput").ap()
    build(nc, out=out, **args)
    result = run_bass_kernel_spmd(nc, [{f"in_{n}": a for n, a in arrays.items()}], core_ids=[0])
    return result.results[0]["out"]
```
